# Optimizing a Trainium2 kernel written in Bass

```python
import numpy as np
import jax
import jax.numpy as jnp

def _softmax(x, axis=-1):
    return jax.nn.softmax(x, axis=axis)

def _gelu(x):
    return jax.nn.gelu(x, approximate=True)

def _silu(x):
    return jax.nn.silu(x)

def _sigmoid(x):
    return jax.nn.sigmoid(x)

def _layernorm(x, axis=-1, eps=1e-05):
    m = jnp.mean(x, axis=axis, keepdims=True)
    v = jnp.var(x, axis=axis, keepdims=True)
    return (x - m) / jnp.sqrt(v + eps)

def _scatter_add(tgt, idx, src, axis=0):
    return tgt.at[idx].add(src)

def _segment_sum(src, seg, n):
    return jax.ops.segment_sum(src, seg, n)
kernel_name = 'mk_gnn_resnorm_d2_gnn_r8_608ab7'

def setup_inputs(seed: int=0):
    np.random.seed(seed)
    _w = jnp.asarray

    def _rec_inputs():
        import jax
        import jax.numpy as jnp
        _gk = jax.random.key(seed)
        x = -8.776e-05 + 1 * jax.random.normal(jax.random.fold_in(_gk, 1), (1250, 512), jnp.float32)
        _s = jax.random.randint(jax.random.fold_in(_gk, 2), (10000,), 0, 1250, jnp.int32)
        _d = jax.random.randint(jax.random.fold_in(_gk, 3), (10000,), 0, 1250, jnp.int32)
        _loop = jnp.arange(1250, dtype=jnp.int32)
        src = jnp.concatenate([_s, _d, _loop])
        dst = jnp.concatenate([_d, _s, _loop])
        _o = jnp.argsort(dst, stable=True)
        src = src[_o]
        dst = dst[_o]
        edge_attr_128 = 0.000279952 + 1.00013 * jax.random.normal(jax.random.fold_in(_gk, 11), (21250, 128), jnp.float32)
        edge_attr_4 = 0.00171547 + 0.999346 * jax.random.normal(jax.random.fold_in(_gk, 12), (21250, 4), jnp.float32)
        edge_attr_8 = 0.000126197 + 0.999763 * jax.random.normal(jax.random.fold_in(_gk, 13), (21250, 8), jnp.float32)
        return (x, src, dst, edge_attr_128, edge_attr_4, edge_attr_8)
    x, src, dst, edge_attr_128, edge_attr_4, edge_attr_8 = _rec_inputs()

    def _L0_gnn_setup():
        import jax, jax.numpy as jnp
        import numpy as np
        MUL = 128
        N_NODES = 1250
        N_EDGES = 20000
        R_BASIS = 8
        HIDDEN = 64
        W_NUMEL = 4 * MUL
        SQRT3 = 3.0 ** 0.5
        SILU_2MOM = 1.679177
        AVG_NUM_NEIGHBORS = 10.0

        def _lin_irreps(x0, x1, W0, W1):
            y0 = x0 @ W0 / jnp.sqrt(jnp.float32(W0.shape[0]))
            y1 = jnp.einsum('num,uv->nvm', x1, W1) / jnp.sqrt(jnp.float32(W1.shape[0]))
            return (y0, y1)

        def _forward(node_feats, edge_attrs, edge_feats, edge_index, W_up0, W_up1, W_mlp1, W_mlp2, W_mlp3, W_mlp4, W_out0, W_out1):
            num_nodes = node_feats.shape[0]
            sender, receiver = (edge_index[0], edge_index[1])
            x0 = node_feats[:, :MUL]
            x1 = node_feats[:, MUL:].reshape(num_nodes, MUL, 3)
            x0, x1 = _lin_irreps(x0, x1, W_up0, W_up1)
            h = edge_feats
            for W in (W_mlp1, W_mlp2, W_mlp3):
                h = SILU_2MOM * jax.nn.silu(h @ W / jnp.sqrt(jnp.float32(W.shape[0])))
            tpw = h @ W_mlp4 / jnp.sqrt(jnp.float32(W_mlp4.shape[0]))
            w1, w2, w3, w4 = jnp.split(tpw, 4, axis=-1)
            s0 = x0[sender]
            s1 = x1[sender]
            y0 = edge_attrs[:, 0:1]
            y1 = edge_attrs[:, 1:4]
            p1 = w1 * s0 * y0
            p2 = (w2 * s0)[:, :, None] * y1[:, None, :]
            p3 = w3[:, :, None] * s1 * y0[:, None, :]
            p4 = w4 * jnp.einsum('eum,em->eu', s1, y1) / SQRT3
            m0 = jnp.concatenate([p1, p4], axis=-1)
            m1 = jnp.concatenate([p2, p3], axis=1)
            msg0 = jax.ops.segment_sum(m0, receiver, num_segments=num_nodes)
            msg1 = jax.ops.segment_sum(m1, receiver, num_segments=num_nodes)
            o0, o1 = _lin_irreps(msg0, msg1, W_out0, W_out1)
            out = jnp.concatenate([o0, o1.reshape(num_nodes, 3 * MUL)], axis=-1)
            return out / AVG_NUM_NEIGHBORS
        key = jax.random.key(seed)
        ks = jax.random.split(key, 12)
        rn = lambda k, s: jax.random.normal(k, s, dtype=jnp.float32)
        return {'node_feats': rn(ks[0], (N_NODES, 4 * MUL)), 'edge_attrs': rn(ks[1], (N_EDGES, 4)), 'edge_feats': rn(ks[2], (N_EDGES, R_BASIS)), 'edge_index': jax.random.randint(ks[3], (2, N_EDGES), 0, N_NODES), 'W_up0': rn(ks[4], (MUL, MUL)), 'W_up1': rn(ks[5], (MUL, MUL)), 'W_mlp1': rn(ks[6], (R_BASIS, HIDDEN)), 'W_mlp2': rn(ks[7], (HIDDEN, HIDDEN)), 'W_mlp3': rn(ks[8], (HIDDEN, HIDDEN)), 'W_mlp4': rn(ks[9], (HIDDEN, W_NUMEL)), 'W_out0': rn(ks[10], (2 * MUL, MUL)), 'W_out1': rn(ks[11], (2 * MUL, MUL))}
    _L0_gnn_all = _L0_gnn_setup()
    _L0_gnn_in = {k: v for k, v in _L0_gnn_all.items() if k in ('W_up0', 'W_up1', 'W_mlp1', 'W_mlp2', 'W_mlp3', 'W_mlp4', 'W_out0', 'W_out1')}
    del _L0_gnn_all

    def _L1_gnn_setup():
        import jax, jax.numpy as jnp
        import numpy as np
        N = 1250
        E = 20000
        D = 512
        EDGE_DIM = 128
        L = 3
        LN_EPS = 1e-05
        key = jax.random.key(seed)
        ks = jax.random.split(key, 16)
        s = 0.02
        return {'x': jax.random.normal(ks[0], (N, D), dtype=jnp.float32), 'edge_index': jax.random.randint(ks[1], (2, E), 0, N, dtype=jnp.int64), 'edge_attr': jax.random.normal(ks[2], (E, EDGE_DIM), dtype=jnp.float32), 'We': jax.random.normal(ks[3], (L, EDGE_DIM, D), dtype=jnp.float32) * s, 'be': jnp.zeros((L, D), dtype=jnp.float32), 'eps': jnp.zeros((L,), dtype=jnp.float32), 'W1': jax.random.normal(ks[4], (L, D, D), dtype=jnp.float32) * s, 'b1': jnp.zeros((L, D), dtype=jnp.float32), 'W2': jax.random.normal(ks[5], (L, D, D), dtype=jnp.float32) * s, 'b2': jnp.zeros((L, D), dtype=jnp.float32), 'gamma': jnp.ones((L, D), dtype=jnp.float32), 'beta': jnp.zeros((L, D), dtype=jnp.float32), 'Wf': jax.random.normal(ks[6], (D, D), dtype=jnp.float32) * s, 'bf': jnp.zeros((D,), dtype=jnp.float32)}
    _L1_gnn_all = _L1_gnn_setup()
    _L1_gnn_in = {k: v for k, v in _L1_gnn_all.items() if k in ('We', 'be', 'eps', 'W1', 'b1', 'W2', 'b2', 'gamma', 'beta', 'Wf', 'bf')}
    del _L1_gnn_all
    return {'x': x, 'src': src, 'dst': dst, 'edge_attr_128': edge_attr_128, 'edge_attr_4': edge_attr_4, 'edge_attr_8': edge_attr_8, 'L0_gnn_W_up0': _L0_gnn_in['W_up0'], 'L0_gnn_W_up1': _L0_gnn_in['W_up1'], 'L0_gnn_W_mlp1': _L0_gnn_in['W_mlp1'], 'L0_gnn_W_mlp2': _L0_gnn_in['W_mlp2'], 'L0_gnn_W_mlp3': _L0_gnn_in['W_mlp3'], 'L0_gnn_W_mlp4': _L0_gnn_in['W_mlp4'], 'L0_gnn_W_out0': _L0_gnn_in['W_out0'], 'L0_gnn_W_out1': _L0_gnn_in['W_out1'], 'L1_gnn_We': _L1_gnn_in['We'], 'L1_gnn_be': _L1_gnn_in['be'], 'L1_gnn_eps': _L1_gnn_in['eps'], 'L1_gnn_W1': _L1_gnn_in['W1'], 'L1_gnn_b1': _L1_gnn_in['b1'], 'L1_gnn_W2': _L1_gnn_in['W2'], 'L1_gnn_b2': _L1_gnn_in['b2'], 'L1_gnn_gamma': _L1_gnn_in['gamma'], 'L1_gnn_beta': _L1_gnn_in['beta'], 'L1_gnn_Wf': _L1_gnn_in['Wf'], 'L1_gnn_bf': _L1_gnn_in['bf']}

def reference(x, src, dst, edge_attr_128, edge_attr_4, edge_attr_8, L0_gnn_W_up0, L0_gnn_W_up1, L0_gnn_W_mlp1, L0_gnn_W_mlp2, L0_gnn_W_mlp3, L0_gnn_W_mlp4, L0_gnn_W_out0, L0_gnn_W_out1, L1_gnn_We, L1_gnn_be, L1_gnn_eps, L1_gnn_W1, L1_gnn_b1, L1_gnn_W2, L1_gnn_b2, L1_gnn_gamma, L1_gnn_beta, L1_gnn_Wf, L1_gnn_bf):
    import jax
    import jax.numpy as jnp

    def _L0_gnn_ref(node_feats, edge_attrs, edge_feats, edge_index, W_up0, W_up1, W_mlp1, W_mlp2, W_mlp3, W_mlp4, W_out0, W_out1):
        import jax, jax.numpy as jnp
        import numpy as np
        MUL = 128
        N_NODES = 1250
        N_EDGES = 20000
        R_BASIS = 8
        HIDDEN = 64
        W_NUMEL = 4 * MUL
        SQRT3 = 3.0 ** 0.5
        SILU_2MOM = 1.679177
        AVG_NUM_NEIGHBORS = 10.0

        def _lin_irreps(x0, x1, W0, W1):
            y0 = x0 @ W0 / jnp.sqrt(jnp.float32(W0.shape[0]))
            y1 = jnp.einsum('num,uv->nvm', x1, W1) / jnp.sqrt(jnp.float32(W1.shape[0]))
            return (y0, y1)

        def _forward(node_feats, edge_attrs, edge_feats, edge_index, W_up0, W_up1, W_mlp1, W_mlp2, W_mlp3, W_mlp4, W_out0, W_out1):
            num_nodes = node_feats.shape[0]
            sender, receiver = (edge_index[0], edge_index[1])
            x0 = node_feats[:, :MUL]
            x1 = node_feats[:, MUL:].reshape(num_nodes, MUL, 3)
            x0, x1 = _lin_irreps(x0, x1, W_up0, W_up1)
            h = edge_feats
            for W in (W_mlp1, W_mlp2, W_mlp3):
                h = SILU_2MOM * jax.nn.silu(h @ W / jnp.sqrt(jnp.float32(W.shape[0])))
            tpw = h @ W_mlp4 / jnp.sqrt(jnp.float32(W_mlp4.shape[0]))
            w1, w2, w3, w4 = jnp.split(tpw, 4, axis=-1)
            s0 = x0[sender]
            s1 = x1[sender]
            y0 = edge_attrs[:, 0:1]
            y1 = edge_attrs[:, 1:4]
            p1 = w1 * s0 * y0
            p2 = (w2 * s0)[:, :, None] * y1[:, None, :]
            p3 = w3[:, :, None] * s1 * y0[:, None, :]
            p4 = w4 * jnp.einsum('eum,em->eu', s1, y1) / SQRT3
            m0 = jnp.concatenate([p1, p4], axis=-1)
            m1 = jnp.concatenate([p2, p3], axis=1)
            msg0 = jax.ops.segment_sum(m0, receiver, num_segments=num_nodes)
            msg1 = jax.ops.segment_sum(m1, receiver, num_segments=num_nodes)
            o0, o1 = _lin_irreps(msg0, msg1, W_out0, W_out1)
            out = jnp.concatenate([o0, o1.reshape(num_nodes, 3 * MUL)], axis=-1)
            return out / AVG_NUM_NEIGHBORS
        return _forward(node_feats, edge_attrs, edge_feats, edge_index, W_up0, W_up1, W_mlp1, W_mlp2, W_mlp3, W_mlp4, W_out0, W_out1)

    def _L1_gnn_ref(x, edge_index, edge_attr, We, be, eps, W1, b1, W2, b2, gamma, beta, Wf, bf):
        import jax, jax.numpy as jnp
        import numpy as np
        N = 1250
        E = 20000
        D = 512
        EDGE_DIM = 128
        L = 3
        LN_EPS = 1e-05
        src = edge_index[0]
        dst = edge_index[1]
        n = x.shape[0]
        h = x
        for l in range(L):
            e = jax.nn.relu(h[src] + edge_attr @ We[l] + be[l])
            agg = jax.ops.segment_sum(e, dst, num_segments=n)
            g = (1.0 + eps[l]) * h + agg
            g = jax.nn.relu(g @ W1[l] + b1[l]) @ W2[l] + b2[l]
            g = jax.nn.relu(g)
            mu = jnp.mean(g, axis=-1, keepdims=True)
            var = jnp.mean(jnp.square(g - mu), axis=-1, keepdims=True)
            h = (g - mu) * jax.lax.rsqrt(var + LN_EPS) * gamma[l] + beta[l]
        return h @ Wf + bf
    edge_index = jnp.stack([src, dst])
    x = _layernorm(x + _L0_gnn_ref(x, edge_attr_4, edge_attr_8, edge_index, L0_gnn_W_up0, L0_gnn_W_up1, L0_gnn_W_mlp1, L0_gnn_W_mlp2, L0_gnn_W_mlp3, L0_gnn_W_mlp4, L0_gnn_W_out0, L0_gnn_W_out1), axis=-1)
    x = _layernorm(x + _L1_gnn_ref(x, edge_index, edge_attr_128, L1_gnn_We, L1_gnn_be, L1_gnn_eps, L1_gnn_W1, L1_gnn_b1, L1_gnn_W2, L1_gnn_b2, L1_gnn_gamma, L1_gnn_beta, L1_gnn_Wf, L1_gnn_bf), axis=-1)
    return x

_drawn_inputs = setup_inputs


def setup_inputs(seed=0):
    import zlib

    import numpy as np

    out = dict(_drawn_inputs(seed))
    spreads = {'L1_gnn_be': (0.0, 0.1),
     'L1_gnn_eps': (0.0, 2.0),
     'L1_gnn_b1': (0.0, 0.397),
     'L1_gnn_b2': (0.0, 0.304),
     'L1_gnn_gamma': (1.0, 0.2),
     'L1_gnn_beta': (0.0, 0.1),
     'L1_gnn_bf': (0.0, 0.1)}
    factors = {'edge_attr_128': 2.921, 'L1_gnn_We': 2.889}
    for name, (base, spread) in spreads.items():
        noise = np.random.default_rng([zlib.crc32(name.encode()), seed]).standard_normal(out[name].shape)
        drawn = base * np.exp(spread * noise) if base else spread * noise
        out[name] = jnp.asarray(drawn.astype(out[name].dtype))
    for name, factor in factors.items():
        out[name] = (out[name] * factor).astype(out[name].dtype)
    return out
```

```python
from contextlib import ExitStack

import concourse.bass as bass
from concourse import mybir

ALU = mybir.AluOpType
ACT = mybir.ActivationFunctionType
AX_X = mybir.AxisListType.X
F32 = mybir.dt.float32
F32R = mybir.dt.float32r
BF16 = mybir.dt.bfloat16
I32 = mybir.dt.int32

P = 128
QT = 4
RT = 3
QE = QT * P
SILU_2MOM = 1.679177
AVG_NEIGHBORS = 10.0
LN_EPS = 1e-5
RANGE_WORDS = 4


def build(nc, x, x_planes, src_t, dst_t, ea_t, ya, ef_t, W_up0, W_up1, W_m1, W_m2, W_m3, W_m4, W_out0, W_out1,
          We, be, be_next, eps, W1, b1, W2, b2, gamma, beta, Wf, bf, out):
    N, D = out.shape
    NT = x.shape[0] // P
    NP = NT * P
    ET = src_t.shape[1]
    NQ = ET // QT
    L = We.shape[0]
    MUL = W_up0.shape[0]
    HID = W_m2.shape[0]
    RB = W_m1.shape[0]
    FC = D // P
    PAIRS = NT // 2
    LAST_ROWS = N - (NT - 1) * P
    assert MUL == P and D == 512 and NT % 2 == 0 and 2 * HID == P and ea_t.shape[0] == P

    table_up = nc.dram_tensor("table_up", (NP, D), F32, kind="Internal").ap()
    table_h = nc.dram_tensor("table_h", (NP, D), F32, kind="Internal").ap()
    ea_parts = nc.dram_tensor("ea_parts", (ET, P, 2 * P), F32, kind="Internal").ap()

    with ExitStack() as ctx:
        def sb(name, shape, dt=F32):
            return ctx.enter_context(nc.sbuf_tensor(name, shape, dt))

        def sem(name):
            return ctx.enter_context(nc.semaphore(name))

        bank = [ctx.enter_context(nc.psum_tensor(f"bank{k}", [P, 512], F32)) for k in range(8)]

        src_idx = sb("src_idx", [P, ET], I32)
        dst_int = sb("dst_int", [P, ET + QT], I32)
        dst_f = sb("dst_f", [P, ET + QT])
        y_attr = sb("y_attr", [P, ET, 4])
        node_iota = sb("node_iota", [P, NP])
        ident = sb("ident", [P, P])
        ones = sb("ones", [P, P])
        zeros = sb("zeros", [P, 512], BF16)
        minus_half = sb("minus_half", [P, 1])
        ranges = sb("ranges", [1, L * NT * RANGE_WORDS], I32)
        h_now = sb("h_now", [P, NT, D])
        h_first = sb("h_first", [P, NT, D])
        sums = sb("sums", [P, NT, 2 * D])
        idx = sb("idx", [P, QT], I32)
        gat = sb("gat", [P, QT, D])
        pre = sb("pre", [P, QT, D])
        e_parts = sb("e_parts", [P, RT, 2, D], F32R)
        e_full = sb("e_full", [P, D])
        ea_slot = sb("ea_slot", [P, QT, 2 * P], F32R)
        hot = sb("hot", [P, QT, P])
        hot_r = sb("hot_r", [P, RT, P], F32R)
        msg = sb("msg", [P, QT, 2 * D])
        w2s = sb("w2s", [P, QT, P])
        dot = sb("dot", [P, QT, P])
        ef_sb = sb("ef_sb", [2 * RB, QE // 2])
        mlp_h = sb("mlp_h", [P, 3, QE // 2])
        x_in = pre[:, 0:2, :]
        xt_in = pre[:, 2:4, :]
        m_in, m_t = msg[:, 0:2, :], msg[:, 2:4, :]
        g_in = msg[:, 0, :].rearrange("p (b n) -> p b n", b=2)
        g_t = msg[:, 1, :].rearrange("p (b n) -> p b n", b=2)
        z_in = msg[:, 2, :].rearrange("p (b n) -> p b n", b=2)
        z_t = msg[:, 3, :].rearrange("p (b n) -> p b n", b=2)
        y_buf = sb("y_buf", [P, 2, D])
        stats = sb("stats", [P, 2, 6])
        mean_var = sb("mean_var", [P, 2, 2])
        var_eps = sb("var_eps", [P, 2])
        rstd = sb("rstd", [P, 2])
        ea_raw = gat[:, 0:2, :]
        ea_split = e_parts[:, 0:2, :, :].rearrange("p b c n -> p b (c n)")
        wup = sb("wup", [P, 2, P])
        wm1 = sb("wm1", [2 * RB, P])
        wm2 = sb("wm2", [P, P])
        wm3 = sb("wm3", [P, P])
        wm4 = sb("wm4", [P, 4 * MUL])
        wo0 = sb("wo0", [P, 2, P])
        wo1 = sb("wo1", [P, 2, P])
        we_raw = sb("we_raw", [P, D])
        we_hi = sb("we_hi", [P, D], F32R)
        we_lo = sb("we_lo", [P, D], F32R)
        w1_sb = sb("w1_sb", [P, FC, D])
        w2_sb = sb("w2_sb", [P, FC, D])
        b1_bc = sb("b1_bc", [P, D])
        b2_bc = sb("b2_bc", [P, D])
        gamma_bc = sb("gamma_bc", [P, D])
        beta_bc = sb("beta_bc", [P, D])
        be_bc = sb("be_bc", [P, D])
        eps_bc = sb("eps_bc", [P, L])
        scratch = h_first[:].rearrange("p a n -> p (a n)")
        taken = [0]

        def carve(n):
            taken[0] += n
            return scratch[:, taken[0] - n:taken[0]]

        ind_flat = carve(NT * ET)
        ind = ind_flat.rearrange("p (a b) -> p a b", a=NT)
        iota_int = carve(NP).bitcast(I32)
        tile_int, tile_f = carve(ET).bitcast(I32), carve(ET)
        q_up, cand = [carve(NT * NQ)[0:1, :].rearrange("p (a b) -> p a b", a=NT) for _ in range(2)]
        q_int = carve(NT * NQ)[0:1, :].bitcast(I32).rearrange("p (a b) -> p a b", a=NT)
        cnt = carve(NT * NQ)[0:1, :]
        rv = sb("rv", [1, 20, NT])
        r_f = sb("r_f", [1, L, NT, RANGE_WORDS])

        s_dst, s_src, s_w0, s_y = sem("dst_loaded"), sem("src_loaded"), sem("weights0_loaded"), sem("y_loaded")
        s_blk, s_wb = sem("blocks_zeroed"), sem("block_weights_loaded")
        s_iota, s_const = sem("iota_made"), sem("consts_made")
        s_ind, s_cnt = sem("indicators_made"), sem("counts_made")
        s_d = sem("dve_chain")
        s_rng = sem("ranges_made")
        s_xt = [sem(f"xt_loaded{b}") for b in range(2)]
        s_up_mm, s_up_ev, s_up_w = sem("up_multiplied"), sem("up_rows_ready"), sem("up_rows_written")
        s_er = [sem(f"ea_raw_loaded{b}") for b in range(2)]
        s_es_hi, s_es_lo = sem("ea_hi_made"), sem("ea_lo_made")
        s_esw = [sem(f"ea_parts_written{b}") for b in range(2)]
        s_ef = sem("ef_loaded")
        s_mlp, s_silu = sem("mlp_multiplied"), sem("silu_done")
        s_tpw = sem("tpw_multiplied")
        s_g0 = [sem(f"first_gathered{j}") for j in range(QT)]
        s_idx0 = sem("first_idx_copied")
        s_msg, s_w2s, s_p2, s_dot = sem("messages_made"), sem("w2s_made"), sem("p2_made"), sem("dot_chain")
        s_hot0, s_b0 = sem("first_hot_made"), sem("first_visited")
        s_acc0 = sem("first_acc_free")
        s_x = [sem(f"x_loaded{b}") for b in range(2)]
        s_mi, s_mtr, s_mt_a, s_mt_d, s_prj = (sem("m_copied"), sem("m_transposed"), sem("mt_saved_act"),
                                              sem("mt_saved_dve"), sem("projected"))
        s_ln0, s_rs0, s_h0, s_h0c, s_rows0 = (sem("first_var_made"), sem("first_rstd_made"), sem("first_h_made"),
                                              sem("first_h_copied"), sem("first_rows_ready"))
        s_n0 = sem("first_chain")
        s_tbl = sem("table_rows_written")
        s_we, s_lw = sem("we_loaded"), sem("layer_weights_loaded")
        s_wsp = sem("we_split")
        s_ea = [sem(f"ea_loaded{j}") for j in range(QT)]
        s_g1 = [sem(f"gathered{j}") for j in range(QT)]
        s_idx1 = sem("idx_copied")
        s_a, s_add, s_hi, s_lo, s_full = (sem("edge_multiplied"), sem("pre_made"), sem("e_hi_made"), sem("e_lo_made"),
                                          sem("e_full_made"))
        s_hot1, s_b1 = sem("hot_made"), sem("visited")
        s_acc1 = sem("acc_free")
        s_gi, s_gtr, s_gt, s_z1, s_zi, s_ztr, s_zt, s_z2 = (
            sem("g_made"), sem("g_transposed"), sem("gt_saved"), sem("w1_multiplied"), sem("z_made"),
            sem("z_transposed"), sem("zt_saved"), sem("w2_multiplied"))
        s_yb, s_yr, s_var, s_rs, s_n1, s_rows = (sem("y_made"), sem("y_relu"), sem("var_made"), sem("rstd_made"),
                                                 sem("node_chain"), sem("rows_ready"))
        s_wf, s_fi, s_ftr, s_ft, s_fm = (sem("wf_loaded"), sem("f_copied"), sem("f_transposed"), sem("ft_saved"),
                                         sem("wf_multiplied"))
        s_fvar, s_frs, s_fn, s_frows, s_out = (sem("f_var_made"), sem("f_rstd_made"), sem("f_chain"),
                                               sem("out_rows_ready"), sem("out_written"))

        block = ctx.enter_context(nc.Block())

        def node_range(eng, row, words):
            low = [0, 1, -L * NT * NQ, 0]
            high = [L * NT * NQ, L * NT * NQ, NQ, ET]
            return [eng.value_load(ranges[0:1, bass.ds(row * RANGE_WORDS + k, 1)], min_val=low[k], max_val=high[k])
                    for k in range(words)]

        def quad_of(step, off):
            return nc.s_assert_within(step + off, 0, NQ - 1,
                                      skip_runtime_bounds_check_because="the ranges are made of quads 0 .. NQ-1")

        def rows_of(table, t):
            return table[bass.ds(t * P, P), :]

        @block.sync
        def _(sp):
            sp.dma_start(dst_int[:], dst_t).then_inc(s_dst, 16)
            sp.dma_start(src_idx[:], src_t).then_inc(s_src, 16)
            sp.dma_start(wup[:, 0, :], W_up0).then_inc(s_w0, 16)
            sp.dma_start(wup[:, 1, :], W_up1).then_inc(s_w0, 16)
            sp.dma_start(wm4[0:HID, :], W_m4).then_inc(s_w0, 16)
            sp.dma_start(wm4[HID:P, :], W_m4).then_inc(s_w0, 16)
            sp.dma_start(wo0[:], W_out0.rearrange("(c p) n -> p c n", p=P)).then_inc(s_w0, 16)
            sp.dma_start(wo1[:], W_out1.rearrange("(c p) n -> p c n", p=P)).then_inc(s_w0, 16)
            sp.dma_start(eps_bc[:], eps.partition_broadcast(P)).then_inc(s_w0, 16)
            sp.dma_start(be_bc[:], be[0].partition_broadcast(P)).then_inc(s_w0, 16)
            sp.dma_start(y_attr[:].rearrange("p t c -> p (t c)"), ya).then_inc(s_y, 16)
            sp.wait_ge(s_blk, 3)
            for g in range(2):
                sp.dma_start(wm1[g * RB:(g + 1) * RB, g * HID:(g + 1) * HID], W_m1).then_inc(s_wb, 16)
                sp.dma_start(wm2[g * HID:(g + 1) * HID, g * HID:(g + 1) * HID], W_m2).then_inc(s_wb, 16)
                sp.dma_start(wm3[g * HID:(g + 1) * HID, g * HID:(g + 1) * HID], W_m3).then_inc(s_wb, 16)

            with sp.Fori(0, PAIRS) as i:
                for b in range(2):
                    t = i * 2 + b
                    sp.wait_ge(s_up_mm, t + 1)
                    sp.nop(nofuse=True)
                    sp.dma_start(xt_in[:, b, :].rearrange("p (c n) -> p c n", c=4),
                                 x_planes[:, :, bass.ds(t * P, P)].rearrange("c u n -> u c n")).then_inc(s_xt[b], 16)
                for b in range(2):
                    t = i * 2 + b
                    sp.wait_ge(s_up_ev, t + 3)
                    sp.nop(nofuse=True)
                    sp.dma_start(rows_of(table_up, t), h_now[:, bass.ds(t, 1), :].rearrange("p a n -> p (a n)")).then_inc(s_up_w, 16)

            with sp.Fori(0, NQ // 2) as i:
                for b in range(2):
                    q = i * 2 + b
                    sp.wait_ge(s_es_lo, q + 1)
                    sp.nop(nofuse=True)
                    sp.dma_start(ea_raw[:, b, :], ea_t[:, bass.ds(q * QE, QE)]).then_inc(s_er[b], 16)
                for b in range(2):
                    q = i * 2 + b
                    sp.wait_ge(s_es_lo, q + 3)
                    sp.nop(nofuse=True)
                    sp.dma_start(ea_parts[bass.ds(q * QT, QT), :, :].rearrange("t p n -> p t n"),
                                 ea_split[:, b, :].bitcast(F32).rearrange("p (t n) -> p t n", t=QT)).then_inc(s_esw[b], 16)

            sp.wait_ge(s_rng, 1)
            with sp.Fori(0, PAIRS) as i:
                for b in range(2):
                    start, end, off = node_range(sp, i * 2 + b, 3)
                    with sp.Fori(start, end) as step:
                        sp.wait_ge(s_mlp, step * 3 + 1)
                        sp.nop(nofuse=True)
                        sp.dma_start(ef_sb[:], ef_t[:, bass.ds(quad_of(step, off) * (QE // 2), QE // 2)]).then_inc(s_ef, 16)
            last_end = sp.value_load(ranges[0:1, (NT - 1) * RANGE_WORDS + 1:(NT - 1) * RANGE_WORDS + 2],
                                     min_val=1, max_val=L * NT * NQ)
            sp.wait_ge(s_mlp, last_end * 3 + 1)
            sp.nop(nofuse=True)
            sp.dma_start(ef_sb[:], ef_t[:, 0:QE // 2]).then_inc(s_ef, 16)

            with sp.Fori(0, PAIRS) as i:
                for b in range(2):
                    t = i * 2 + b
                    sp.wait_ge(s_h0, t + 1)
                    sp.nop(nofuse=True)
                    sp.dma_start(x_in[:, b, :], rows_of(x, t)).then_inc(s_x[b], 16)
                for b in range(2):
                    t = i * 2 + b
                    sp.wait_ge(s_rows0, t + 1)
                    sp.nop(nofuse=True)
                    sp.dma_start(rows_of(table_h, t), sums[:, bass.ds(t, 1), 0:D].rearrange("p a n -> p (a n)")).then_inc(s_tbl, 16)

            for b in range(2):
                sp.wait_ge(s_esw[b], 16 * (NQ // 2))
            with sp.Fori(0, L) as l:
                sp.wait_ge(s_rows, l * NT + 1)
                sp.nop(nofuse=True)
                sp.dma_start(we_raw[:], We[bass.ds(l, 1), :, :].rearrange("a k n -> k (a n)")).then_inc(s_we, 16)
                sp.dma_start(w1_sb[:], W1[bass.ds(l, 1), :, :].rearrange("a (c p) n -> p (a c) n", p=P)).then_inc(s_lw, 16)
                sp.dma_start(w2_sb[:], W2[bass.ds(l, 1), :, :].rearrange("a (c p) n -> p (a c) n", p=P)).then_inc(s_lw, 16)
                for tile, rows in ((b1_bc, b1), (b2_bc, b2), (gamma_bc, gamma), (beta_bc, beta), (be_bc, be_next)):
                    sp.dma_start(tile[:], rows[bass.ds(l, 1), :].rearrange("a n -> (a n)").partition_broadcast(P)).then_inc(s_lw, 16)
                with sp.Fori(0, PAIRS) as i:
                    for b in range(2):
                        start, end, off = node_range(sp, l * NT + i * 2 + b, 3)
                        with sp.Fori(start, end) as step:
                            for j in range(QT):
                                sp.wait_ge(s_a, step * QT + j + 1)
                                sp.nop(nofuse=True)
                                sp.dma_start(ea_slot[:, j, :].bitcast(F32), ea_parts[bass.ds(quad_of(step, off) * QT + j, 1), :, :]
                                             .rearrange("t p n -> p (t n)")).then_inc(s_ea[j], 16)
                with sp.Fori(0, NT) as t:
                    sp.wait_ge(s_rows, l * NT + t + 2)
                    sp.nop(nofuse=True)
                    sp.dma_start(rows_of(table_h, t), sums[:, bass.ds(t, 1), D:2 * D].rearrange("p a n -> p (a n)")).then_inc(s_tbl, 16)

            sp.dma_start(w1_sb[:], Wf.rearrange("(c p) n -> p c n", p=P)).then_inc(s_wf, 16)
            sp.dma_start(b1_bc[:], bf.partition_broadcast(P)).then_inc(s_wf, 16)
            with sp.Fori(0, NT - 1) as t:
                sp.wait_ge(s_frows, t + 3)
                sp.nop(nofuse=True)
                sp.dma_start(rows_of(out, t), sums[:, bass.ds(t, 1), 0:D].rearrange("p a n -> p (a n)")).then_inc(s_out, 16)
            sp.wait_ge(s_frows, NT + 2)
            sp.dma_start(out[(NT - 1) * P:N, :], sums[0:LAST_ROWS, NT - 1, 0:D]).then_inc(s_out, 16)
            sp.wait_ge(s_out, 16 * NT)
            sp.wait_ge(s_up_w, 16 * NT)
            sp.wait_ge(s_tbl, 16 * NT * (L + 1))

        @block.gpsimd
        def _(pool):
            nc.gpsimd.iota(iota_int, [[1, NP]], base=0, channel_multiplier=0).then_inc(s_iota, 1)
            nc.gpsimd.iota(q_int, [[0, NT], [1, NQ]], base=1, channel_multiplier=0).then_inc(s_iota, 1)
            nc.gpsimd.memset(ones[:], 1.0).then_inc(s_const, 1)
            nc.gpsimd.memset(zeros[:], 0.0).then_inc(s_const, 1)
            nc.gpsimd.memset(minus_half[:], -0.5).then_inc(s_const, 1)
            pool.wait_ge(s_const, 3)
            nc.gpsimd.affine_select(out=ident[:], in_=ones[:], compare_op=ALU.is_equal, fill=0.0, base=0,
                                    pattern=[[-1, P]], channel_multiplier=1).then_inc(s_const, 1)

            def gather(table, column, count, j, freed, copied, landed):
                pool.wait_ge(freed, count + j + 1)
                nc.gpsimd.tensor_copy(idx[:, j:j + 1], src_idx[:, bass.ds(column + j, 1)]).then_inc(copied, 1)
                pool.wait_ge(copied, count + j + 1)
                pool.nop(nofuse=True)
                pool.indirect_dma_start(out=gat[:, j, :], out_offset=None, in_=table,
                                        in_offset=bass.IndirectOffsetOnAxis(ap=idx[:, j:j + 1], axis=0)
                                        ).then_inc(landed[j], 16)

            pool.wait_ge(s_rng, 1)
            pool.wait_ge(s_src, 16)
            pool.wait_ge(s_up_w, 16 * NT)
            pool.wait_ge(s_es_lo, NQ + 2)
            pool.wait_ge(s_es_hi, NQ)
            with pool.Fori(0, PAIRS) as i:
                for b in range(2):
                    start, end, off = node_range(pool, i * 2 + b, 3)
                    with pool.Fori(start, end) as step:
                        for j in range(QT):
                            gather(table_up, quad_of(step, off) * QT, step * QT, j, s_msg, s_idx0, s_g0)

            pool.wait_ge(s_acc0, NT + 2)
            with pool.Fori(0, PAIRS) as i:
                for b in range(2):
                    t = i * 2 + b
                    pool.wait_ge(s_mtr, t + 1)
                    nc.gpsimd.tensor_copy(m_in[:, b, :], sums[:, bass.ds(t, 1), :].rearrange("p a n -> p (a n)")).then_inc(s_mi, 1)
                for b in range(2):
                    t = i * 2 + b
                    pool.wait_ge(s_ln0, t + 1)
                    nc.gpsimd.tensor_tensor(rstd[:, b:b + 1], var_eps[:, b:b + 1], minus_half[:], ALU.pow).then_inc(s_rs0, 1)
                    pool.wait_ge(s_h0, t + 3)
                    nc.gpsimd.tensor_copy(h_first[:, bass.ds(t, 1), :], h_now[:, bass.ds(t, 1), :]).then_inc(s_h0c, 1)

            with pool.Fori(0, L) as l:
                pool.wait_ge(s_tbl, (l + 1) * (16 * NT))
                pool.nop(nofuse=True)
                with pool.Fori(0, PAIRS) as i:
                    for b in range(2):
                        start, end, off = node_range(pool, l * NT + i * 2 + b, 3)
                        with pool.Fori(start, end) as step:
                            for j in range(QT):
                                gather(table_h, quad_of(step, off) * QT, step * QT, j, s_add, s_idx1, s_g1)
                with pool.Fori(0, PAIRS) as i:
                    for b in range(2):
                        pool.wait_ge(s_var, l * NT + i * 2 + b + 1)
                        nc.gpsimd.tensor_tensor(rstd[:, b:b + 1], var_eps[:, b:b + 1], minus_half[:], ALU.pow).then_inc(s_rs, 1)

            pool.wait_ge(s_rows, L * NT + 1)
            with pool.Fori(0, PAIRS) as i:
                for b in range(2):
                    t = i * 2 + b
                    pool.wait_ge(s_ftr, t + 1)
                    nc.gpsimd.tensor_copy(g_in[:, b, :], h_now[:, bass.ds(t, 1), :].rearrange("p a n -> p (a n)")).then_inc(s_fi, 1)
                for b in range(2):
                    pool.wait_ge(s_fvar, i * 2 + b + 3)
                    nc.gpsimd.tensor_tensor(rstd[:, b:b + 1], var_eps[:, b:b + 1], minus_half[:], ALU.pow).then_inc(s_frs, 1)

        @block.tensor
        def _(pe):
            pe.wait_ge(s_ind, NT)
            pe.wait_ge(s_const, 4)
            for k in range(4):
                w = NT * ET // 4
                nc.tensor.matmul(bank[k][0:1, 0:w], ones[:, 0:1], ind_flat[:, k * w:(k + 1) * w],
                                 start=True, stop=True).then_inc(s_cnt, 1)

            pe.wait_ge(s_w0, 16 * 8)
            with pe.Fori(0, PAIRS) as i:
                for b in range(2):
                    t = i * 2 + b
                    pe.wait_ge(s_xt[b], i * 16 + 16)
                    pe.wait_ge(s_up_ev, t + 1)
                    for c in range(4):
                        last = nc.tensor.matmul(bank[4 + b][:, c * P:(c + 1) * P], xt_in[:, b, c * P:(c + 1) * P],
                                                wup[:, min(c, 1), :], start=True, stop=True)
                    last.then_inc(s_up_mm, 1)

            def mlp(layer, at):
                if layer == 0:
                    pe.wait_ge(s_ef, at * 16 + 16)
                pe.wait_ge(s_silu, at * 3 + 3 + layer)
                w = (wm1, wm2, wm3)[layer]
                rhs = ef_sb[:] if layer == 0 else mlp_h[:, layer - 1, :]
                nc.tensor.matmul(bank[2 + layer % 2][:, 0:QE // 2], w[:], rhs, start=True, stop=True).then_inc(s_mlp, 1)

            def visit_first(b, j, step, count, stop):
                pe.wait_ge(s_msg, step * QT + j + 1)
                pe.wait_ge(s_p2, step * QT + j + 1)
                pe.wait_ge(s_hot0, count * QT + j + 1)
                for c in range(2):
                    last = nc.tensor.matmul(bank[4 + 2 * b + c][:, :], hot[:, j, :], msg[:, j, c * D:(c + 1) * D],
                                            start=False, stop=stop)
                last.then_inc(s_b0, 1)

            def open_sums(banks):
                for k in banks:
                    nc.tensor.matmul(bank[k][:, :], zeros[:, 0:P], zeros[:, :], start=True, stop=False)

            pe.wait_ge(s_wb, 16 * 6)
            pe.wait_ge(s_up_ev, NT + 2)
            pe.wait_ge(s_rng, 1)
            for layer in range(3):
                mlp(layer, 0)
            with pe.Fori(0, PAIRS) as i:
                for b in range(2):
                    t = i * 2 + b
                    start, end = node_range(pe, t, 2)
                    pe.wait_ge(s_acc0, t + 1)
                    open_sums((4 + 2 * b, 5 + 2 * b))
                    with pe.Fori(start, end) as step:
                        for j in range(QT):
                            g, half = j // 2, j % 2
                            if j == 0:
                                pe.wait_ge(s_silu, step * 3 + 6)
                            pe.wait_ge(s_msg, step * QT + j + 3)
                            nc.tensor.matmul(bank[j % 2][:, :], mlp_h[g * HID:(g + 1) * HID, 2, half * P:(half + 1) * P],
                                             wm4[g * HID:(g + 1) * HID, :], start=True, stop=True).then_inc(s_tpw, 1)
                            visit_first(b, j, step, step + t, False)
                            if j < 3:
                                mlp(j, step + 1)
                    for j in range(QT):
                        visit_first(b, j, end, end + t, j == QT - 1)

            pe.wait_ge(s_acc0, NT + 2)
            with pe.Fori(0, PAIRS) as i:
                for b in range(2):
                    t = i * 2 + b
                    pe.wait_ge(s_mi, t + 1)
                    for c in range(8):
                        last = nc.tensor.transpose(bank[2 * b + c // 4][:, (c % 4) * P:(c % 4 + 1) * P],
                                                   m_in[:, b, c * P:(c + 1) * P], ident[:])
                    last.then_inc(s_mtr, 1)
                for b in range(2):
                    t = i * 2 + b
                    pe.wait_ge(s_mt_a, t + 1)
                    pe.wait_ge(s_mt_d, t + 1)
                    pe.wait_ge(s_h0, t + 1)
                    pairs = [(0, 0, wo0, 0), (0, 1, wo0, 1)]
                    for m in range(3):
                        pairs += [(1 + m, 2 + m, wo1, 0), (1 + m, 5 + m, wo1, 1)]
                    for o, c, w, half in pairs:
                        last = nc.tensor.matmul(bank[4 + b][:, o * P:(o + 1) * P], m_t[:, b, c * P:(c + 1) * P],
                                                w[:, half, :], start=(half == 0), stop=(half == 1))
                    last.then_inc(s_prj, 1)

            def visit(b, j, step, count, stop):
                pe.wait_ge(s_hot1, count * QT + j + 1)
                if j < RT:
                    pe.wait_ge(s_lo, step * RT + j + 1)
                    nc.tensor.matmul(bank[4 + b][:, :], hot_r[:, j, :], e_parts[:, j, 1, :], start=False, stop=False)
                    last = nc.tensor.matmul(bank[4 + b][:, :], hot_r[:, j, :], e_parts[:, j, 0, :], start=False, stop=stop)
                else:
                    pe.wait_ge(s_full, step + 1)
                    last = nc.tensor.matmul(bank[4 + b][:, :], hot[:, j, :], e_full[:], start=False, stop=stop)
                last.then_inc(s_b1, 1)

            def transposes(dst_bank, source, done):
                for c in range(FC):
                    last = nc.tensor.transpose(bank[dst_bank][:, c * P:(c + 1) * P], source[:, c * P:(c + 1) * P], ident[:])
                last.then_inc(done, 1)

            def dense(dst_bank, source_t, w, done):
                for c in range(FC):
                    last = nc.tensor.matmul(bank[dst_bank][:, :], source_t[:, c * P:(c + 1) * P], w[:, c, :],
                                            start=(c == 0), stop=(c == FC - 1))
                last.then_inc(done, 1)

            pe.wait_ge(s_h0, NT + 2)
            with pe.Fori(0, L) as l:
                pe.wait_ge(s_wsp, l * 2 + 2)
                pe.wait_ge(s_rows, l * NT + 1)
                pe.nop(nofuse=True)
                with pe.Fori(0, PAIRS) as i:
                    for b in range(2):
                        t = l * NT + i * 2 + b
                        start, end = node_range(pe, t, 2)
                        pe.wait_ge(s_acc1, t + 1)
                        open_sums((4 + b,))
                        with pe.Fori(start, end) as step:
                            for j in range(QT):
                                pe.wait_ge(s_ea[j], step * 16 + 16)
                                pe.wait_ge(s_add, step * QT + j + 1)
                                for k, (a, w) in enumerate(((1, we_hi), (0, we_lo), (0, we_hi))):
                                    last = nc.tensor.matmul(bank[j][:, :], ea_slot[:, j, a * P:(a + 1) * P], w[:],
                                                            start=(k == 0), stop=(k == 2))
                                last.then_inc(s_a, 1)
                                visit(b, j, step, step + t, False)
                        for j in range(QT):
                            visit(b, j, end, end + t, j == QT - 1)

                pe.wait_ge(s_lw, l * (16 * 7) + 16 * 7)
                pe.nop(nofuse=True)
                with pe.Fori(0, PAIRS) as i:
                    n = [l * NT + i * 2 + b for b in range(2)]
                    for b in range(2):
                        pe.wait_ge(s_gi, n[b] + 1)
                        transposes(b, g_in[:, b, :], s_gtr)
                    for b in range(2):
                        pe.wait_ge(s_gt, n[b] + 1)
                        dense(2 + b, g_t[:, b, :], w1_sb, s_z1)
                    for b in range(2):
                        pe.wait_ge(s_zi, n[b] + 1)
                        transposes(b, z_in[:, b, :], s_ztr)
                    for b in range(2):
                        pe.wait_ge(s_zt, n[b] + 1)
                        pe.wait_ge(s_yb, n[b] + 1)
                        dense(6 + b, z_t[:, b, :], w2_sb, s_z2)

            pe.wait_ge(s_wf, 32)
            with pe.Fori(0, PAIRS) as i:
                for b in range(2):
                    pe.wait_ge(s_fi, i * 2 + b + 1)
                    transposes(b, g_in[:, b, :], s_ftr)
                for b in range(2):
                    pe.wait_ge(s_ft, i * 2 + b + 1)
                    pe.wait_ge(s_fvar, i * 2 + b + 1)
                    dense(2 + b, g_t[:, b, :], w1_sb, s_fm)

        @block.scalar
        def _(act):
            with act.Fori(0, PAIRS) as i:
                for b in range(2):
                    t = i * 2 + b
                    act.wait_ge(s_up_mm, t + 3)
                    nc.scalar.activation(h_now[:, bass.ds(t, 1), :].rearrange("p a n -> p (a n)"), bank[4 + b][:, :],
                                         ACT.Copy, scale=float(MUL) ** -0.5).then_inc(s_up_ev, 1)
            def high_part(b):
                nc.scalar.copy(ea_split[:, b, :].rearrange("p (t c n) -> p t c n", t=QT, c=2)[:, :, 0, :],
                               ea_raw[:, b, :].rearrange("p (t n) -> p t n", t=QT)).then_inc(s_es_hi, 1)

            for b in range(2):
                act.wait_ge(s_er[b], 16)
                high_part(b)
            with act.Fori(1, NQ // 2) as i:
                for b in range(2):
                    act.wait_ge(s_er[b], i * 16 + 16)
                    act.wait_ge(s_esw[b], i * 16)
                    high_part(b)

            def silu(layer, at):
                act.wait_ge(s_mlp, at * 3 + 4 + layer)
                if layer == 2:
                    act.wait_ge(s_tpw, at * QT + QT)
                scale = float(RB) ** -0.5 if layer == 0 else SILU_2MOM * float(HID) ** -0.5
                nc.scalar.activation(mlp_h[:, layer, :], bank[2 + layer % 2][:, 0:QE // 2], ACT.Silu,
                                     scale=scale).then_inc(s_silu, 1)

            for layer in range(3):
                silu(layer, 0)
            with act.Fori(0, PAIRS) as i:
                for b in range(2):
                    t = i * 2 + b
                    start, end, off = node_range(act, t, 3)
                    with act.Fori(start, end) as step:
                        for j in range(QT):
                            act.wait_ge(s_w2s, step * QT + j + 1)
                            act.wait_ge(s_b0, (step + t) * QT + j + 5)
                            for m in range(3):
                                last = nc.scalar.mul(msg[:, j, (2 + m) * P:(3 + m) * P], w2s[:, j, :],
                                                     y_attr[:, bass.ds(quad_of(step, off) * QT + j, 1), 1 + m:2 + m]
                                                     .rearrange("p a c -> p (a c)"))
                            last.then_inc(s_p2, 1)
                            if j < 3:
                                silu(j, step + 1)
                    act.wait_ge(s_b0, (end + t) * QT + 8)
                    for c in range(2):
                        last = nc.scalar.copy(sums[:, bass.ds(t, 1), c * D:(c + 1) * D].rearrange("p a n -> p (a n)"),
                                              bank[4 + 2 * b + c][:, :])
                    last.then_inc(s_acc0, 1)

            with act.Fori(0, PAIRS) as i:
                for b in range(2):
                    t = i * 2 + b
                    act.wait_ge(s_mtr, t + 3)
                    act.wait_ge(s_prj, t + 1)
                    nc.scalar.copy(m_t[:, b, 0:D], bank[2 * b][:, :]).then_inc(s_mt_a, 1)

            with act.Fori(0, L) as l:
                with act.Fori(0, PAIRS) as i:
                    for b in range(2):
                        t = l * NT + i * 2 + b
                        start, end = node_range(act, t, 2)
                        with act.Fori(start, end) as step:
                            for j in range(QT):
                                act.wait_ge(s_add, step * QT + j + 1 + QT)
                                act.wait_ge(s_b1, (step + t) * QT + j + 5)
                                if j < RT:
                                    nc.scalar.activation(e_parts[:, j, 0, :], pre[:, j, :], ACT.Relu).then_inc(s_hi, 1)
                                else:
                                    nc.scalar.activation(e_full[:], pre[:, j, :], ACT.Relu).then_inc(s_full, 1)
                        act.wait_ge(s_b1, (end + t) * QT + 8)
                        nc.scalar.copy(sums[:, bass.ds(i * 2 + b, 1), 0:D].rearrange("p a n -> p (a n)"),
                                       bank[4 + b][:, :]).then_inc(s_acc1, 1)
                with act.Fori(0, PAIRS) as i:
                    n = [l * NT + i * 2 + b for b in range(2)]
                    for b in range(2):
                        act.wait_ge(s_gtr, n[b] + 1)
                        nc.scalar.copy(g_t[:, b, :], bank[b][:, :]).then_inc(s_gt, 1)
                    for b in range(2):
                        act.wait_ge(s_ztr, n[b] + 1)
                        nc.scalar.activation(z_t[:, b, :], bank[b][:, :], ACT.Relu).then_inc(s_zt, 1)
                    for b in range(2):
                        act.wait_ge(s_yb, n[b] + 3)
                        nc.scalar.activation(y_buf[:, b, :], y_buf[:, b, :], ACT.Relu).then_inc(s_yr, 1)

            with act.Fori(0, PAIRS) as i:
                for b in range(2):
                    act.wait_ge(s_ftr, i * 2 + b + 3)
                    nc.scalar.copy(g_t[:, b, :], bank[b][:, :]).then_inc(s_ft, 1)

        @block.vector
        def _(dve):
            chain = [0]

            def link(ins):
                chain[0] += 1
                ins.then_inc(s_d, 1)
                dve.wait_ge(s_d, chain[0])

            V = nc.vector
            for k, w in enumerate((wm1, wm2, wm3)):
                V.memset(w[:], 0.0).then_inc(s_blk, 1)
            V.memset(msg[:], 0.0).then_inc(s_msg, QT)
            V.memset(e_full[:], 0.0).then_inc(s_full, 1)
            for s, n in ((s_up_mm, 2), (s_up_ev, 2), (s_es_lo, 2), (s_mlp, 3), (s_silu, 3), (s_tpw, QT),
                         (s_p2, QT), (s_b0, QT), (s_acc0, 2), (s_mtr, 2), (s_prj, 2), (s_h0, 2), (s_rows, 1), (s_a, QT),
                         (s_add, QT), (s_b1, QT), (s_acc1, 2), (s_yb, 2), (s_ftr, 2), (s_fvar, 2), (s_frows, 2)):
                dve.sem_inc(s, n)

            dve.wait_ge(s_iota, 2)
            link(V.tensor_copy(node_iota[:], iota_int))
            link(V.tensor_copy(q_up, q_int))
            dve.wait_ge(s_dst, 16)
            link(V.tensor_copy(dst_f[:], dst_int[:]))
            link(V.tensor_scalar(tile_int, dst_int[:, 0:ET], P.bit_length() - 1, None, ALU.arith_shift_right))
            link(V.tensor_copy(tile_f, tile_int))
            for t in range(NT):
                V.tensor_scalar(ind[:, t, :], tile_f, float(t), None, ALU.is_equal).then_inc(s_ind, 1)
            for k in range(4):
                w = NT * ET // 4
                dve.wait_ge(s_cnt, k + 1)
                link(V.tensor_reduce(cnt[0:1, k * w // QT:(k + 1) * w // QT],
                                     bank[k][0:1, 0:w].rearrange("p (q j) -> p q j", j=QT), AX_X, ALU.add))
            (has, first, last, lo, hi, carry, flag, gt, start, count, cum, end, off, ccol, keep, cum1, prev, tmp, hn, ln) = \
                [rv[0:1, k, :] for k in range(20)]
            held = cnt.rearrange("p (t q) -> p t q", t=NT)
            link(V.tensor_scalar(held, held, 1.0, None, ALU.min))
            link(V.tensor_reduce(has, held, AX_X, ALU.max))
            link(V.tensor_tensor(cand, held, q_up, ALU.mult))
            link(V.tensor_reduce(last, cand, AX_X, ALU.max))
            link(V.tensor_scalar(last, last, -1.0, None, ALU.add))
            link(V.tensor_scalar(q_up, q_up, -1.0, float(NQ + 1), ALU.mult, ALU.add))
            link(V.tensor_tensor(cand, held, q_up, ALU.mult))
            link(V.tensor_reduce(first, cand, AX_X, ALU.max))
            link(V.tensor_scalar(first, first, -1.0, float(NQ), ALU.mult, ALU.add))
            link(V.tensor_scalar(keep, has, -1.0, 1.0, ALU.mult, ALU.add))
            link(V.tensor_tensor(hn, has, last, ALU.mult))
            link(V.tensor_tensor_scan(hi, keep, hn, 0.0, ALU.mult, ALU.add))
            link(V.memset(carry, 0.0))
            link(V.tensor_copy(carry[:, 1:NT], hi[:, 0:NT - 1]))
            link(V.tensor_tensor(ln, has, first, ALU.mult))
            link(V.tensor_tensor(tmp, keep, carry, ALU.mult))
            link(V.tensor_tensor(lo, ln, tmp, ALU.add))
            link(V.tensor_tensor(flag, lo, carry, ALU.is_equal))
            link(V.tensor_tensor(gt, hi, carry, ALU.is_gt))
            link(V.tensor_tensor(flag, flag, gt, ALU.mult))
            link(V.memset(flag[:, 0:1], 0.0))
            link(V.tensor_tensor(start, lo, flag, ALU.add))
            link(V.tensor_tensor(count, hi, start, ALU.subtract))
            link(V.tensor_scalar(count, count, 1.0, None, ALU.add))
            link(V.memset(keep, 1.0))
            link(V.tensor_tensor_scan(end, keep, count, 0.0, ALU.mult, ALU.add))
            link(V.tensor_tensor(cum, end, count, ALU.subtract))
            link(V.tensor_scalar(ccol, carry, float(QT), float(-ET), ALU.mult, ALU.add))
            link(V.tensor_tensor(ccol, ccol, flag, ALU.mult))
            link(V.tensor_scalar(ccol, ccol, float(ET), None, ALU.add))
            for l in range(L):
                if l:
                    link(V.tensor_scalar(cum, cum, end_total, None, ALU.add))
                    link(V.tensor_scalar(end, end, end_total, None, ALU.add))
                else:
                    end_total = prev[:, 0:1]
                    link(V.tensor_copy(end_total, end[:, NT - 1:NT]))
                link(V.tensor_copy(r_f[:, l, :, 0], cum))
                link(V.tensor_copy(r_f[:, l, :, 1], end))
                link(V.tensor_tensor(r_f[:, l, :, 2], start, cum, ALU.subtract))
                link(V.tensor_copy(r_f[:, l, :, 3], ccol))
            V.tensor_copy(ranges[:], r_f[:].rearrange("p l t k -> p (l t k)")).then_inc(s_rng, 1)
            dve.wait_ge(s_y, 16)
            link(V.tensor_scalar(y_attr[:], y_attr[:], SILU_2MOM * float(HID) ** -0.5, None, ALU.mult))
            dve.wait_ge(s_w0, 16 * 8)
            link(V.tensor_scalar(wo0[:, 1, :], wo0[:, 1, :], 3.0 ** -0.5, None, ALU.mult))
            link(V.tensor_scalar(eps_bc[:], eps_bc[:], 1.0, None, ALU.add))

            with dve.Fori(0, NQ // 2) as i:
                for b in range(2):
                    q = i * 2 + b
                    parts = ea_split[:, b, :].rearrange("p (t c n) -> p t c n", t=QT, c=2)
                    dve.wait_ge(s_es_hi, q + 1)
                    V.tensor_tensor(parts[:, :, 1, :], ea_raw[:, b, :].rearrange("p (t n) -> p t n", t=QT),
                                    parts[:, :, 0, :].bitcast(F32), ALU.subtract).then_inc(s_es_lo, 1)

            def one_hot(target, column, t, done):
                V.tensor_scalar(target, node_iota[:, bass.ds(t * P, P)], dst_f[:, bass.ds(column, 1)], None,
                                ALU.is_equal).then_inc(done, 1)

            dve.wait_ge(s_rng, 1)
            with dve.Fori(0, PAIRS) as i:
                for b in range(2):
                    t = i * 2 + b
                    start, end, off, carried = node_range(dve, t, 4)
                    for j in range(QT):
                        dve.wait_ge(s_b0, (start + t) * QT + j + 1)
                        one_hot(hot[:, j, :], carried + j, t, s_hot0)
                    with dve.Fori(start, end) as step:
                        for j in range(QT):
                            tile = step * QT + j
                            column = quad_of(step, off) * QT + j
                            y = [y_attr[:, bass.ds(column, 1), k:k + 1].rearrange("p a c -> p (a c)") for k in range(4)]
                            s = [gat[:, j, k * P:(k + 1) * P] for k in range(4)]
                            w = [bank[j % 2][:, k * P:(k + 1) * P] for k in range(4)]
                            dot_j = dot[:, j, :]
                            dve.wait_ge(s_g0[j], step * 16 + 16)
                            V.tensor_scalar(dot_j, s[1], y[1], None, ALU.mult).then_inc(s_dot, 1)
                            dve.wait_ge(s_tpw, tile + 1 + QT)
                            dve.wait_ge(s_p2, tile + 1)
                            V.tensor_tensor(w2s[:, j, :], w[1], s[0], ALU.mult).then_inc(s_w2s, 1)
                            dve.wait_ge(s_dot, tile * 3 + 1)
                            V.scalar_tensor_tensor(dot_j, s[2], y[2], dot_j, ALU.mult, ALU.add).then_inc(s_dot, 1)
                            dve.wait_ge(s_b0, (step + t) * QT + j + 5)
                            one_hot(hot[:, j, :], column, t, s_hot0)
                            V.scalar_tensor_tensor(msg[:, j, 0:P], w[0], y[0], s[0], ALU.mult, ALU.mult)
                            dve.wait_ge(s_dot, tile * 3 + 2)
                            V.scalar_tensor_tensor(dot_j, s[3], y[3], dot_j, ALU.mult, ALU.add).then_inc(s_dot, 1)
                            dve.wait_ge(s_dot, tile * 3 + 3)
                            V.tensor_tensor(msg[:, j, P:2 * P], w[3], dot_j, ALU.mult)
                            V.scalar_tensor_tensor(msg[:, j, 5 * P:8 * P].rearrange("p (m u) -> p m u", m=3),
                                                   w[2].unsqueeze(1).to_broadcast([P, 3, P]), y[0],
                                                   gat[:, j, P:4 * P].rearrange("p (m u) -> p m u", m=3),
                                                   ALU.mult, ALU.mult).then_inc(s_msg, 1)

            def row_stats(b, source, c, counter, base, var_done):
                V.bn_stats(stats[:, b, :], source).then_inc(counter, 1)
                dve.wait_ge(counter, base + 1)
                dve.nop(nofuse=True)
                V.bn_aggr(mean_var[:, b, :], stats[:, b, :]).then_inc(counter, 1)
                dve.wait_ge(counter, base + 2)
                V.tensor_scalar(var_eps[:, b:b + 1], mean_var[:, b, 1:2], LN_EPS, None, ALU.add).then_inc(var_done, 1)

            with dve.Fori(0, PAIRS) as i:
                for b in range(2):
                    t = i * 2 + b
                    dve.wait_ge(s_mtr, t + 3)
                    dve.wait_ge(s_prj, t + 1)
                    V.tensor_copy(m_t[:, b, D:2 * D], bank[2 * b + 1][:, :]).then_inc(s_mt_d, 1)
                for b in range(2):
                    t = i * 2 + b
                    scale = (2.0 * MUL) ** -0.5 / AVG_NEIGHBORS
                    dve.wait_ge(s_prj, t + 3)
                    dve.wait_ge(s_x[b], i * 16 + 16)
                    V.scalar_tensor_tensor(y_buf[:, b, 0:P], bank[4 + b][:, 0:P], scale, x_in[:, b, 0:P],
                                           ALU.mult, ALU.add).then_inc(s_n0, 1)
                    V.scalar_tensor_tensor(y_buf[:, b, P:D].rearrange("p (v m) -> p m v", m=3),
                                           bank[4 + b][:, P:D].rearrange("p (m v) -> p m v", m=3), scale,
                                           x_in[:, b, P:D].rearrange("p (v m) -> p m v", m=3),
                                           ALU.mult, ALU.add).then_inc(s_n0, 1)
                    dve.wait_ge(s_n0, t * 4 + 2)
                    row_stats(b, y_buf[:, b, :], t, s_n0, t * 4 + 2, s_ln0)
                for b in range(2):
                    t = i * 2 + b
                    now = h_now[:, bass.ds(t, 1), :].rearrange("p a n -> p (a n)")
                    dve.wait_ge(s_rs0, t + 1)
                    V.tensor_scalar(now, y_buf[:, b, :], mean_var[:, b, 0:1], rstd[:, b:b + 1],
                                    ALU.subtract, ALU.mult).then_inc(s_h0, 1)
                    dve.wait_ge(s_h0, t + 3)
                    dve.wait_ge(s_mi, t + 1)
                    V.tensor_tensor(sums[:, bass.ds(t, 1), 0:D].rearrange("p a n -> p (a n)"), now, be_bc[:],
                                    ALU.add).then_inc(s_rows0, 1)

            for b in range(2):
                dve.wait_ge(s_esw[b], 16 * (NQ // 2))
            V.memset(e_parts[:].rearrange("p a c n -> p (a c n)").bitcast(F32), 0.0).then_inc(s_lo, RT)
            with dve.Fori(0, L) as l:
                dve.wait_ge(s_we, l * 16 + 16)
                V.tensor_copy(we_hi[:], we_raw[:]).then_inc(s_wsp, 1)
                dve.wait_ge(s_wsp, l * 2 + 1)
                V.tensor_tensor(we_lo[:], we_raw[:], we_hi[:].bitcast(F32), ALU.subtract).then_inc(s_wsp, 1)
                with dve.Fori(0, PAIRS) as i:
                    for b in range(2):
                        node_tile = i * 2 + b
                        t = l * NT + node_tile
                        start, end, off, carried = node_range(dve, t, 4)

                        def hot_slot(j):
                            return hot_r[:, j, :] if j < RT else hot[:, j, :]

                        for j in range(QT):
                            dve.wait_ge(s_b1, (start + t) * QT + j + 1)
                            one_hot(hot_slot(j), carried + j, node_tile, s_hot1)
                        with dve.Fori(start, end) as step:
                            def low_part(j):
                                dve.wait_ge(s_hi, step * RT + j + 1)
                                V.scalar_tensor_tensor(e_parts[:, j, 1, :], pre[:, j, :], 0.0,
                                                       e_parts[:, j, 0, :].bitcast(F32), ALU.max,
                                                       ALU.subtract).then_inc(s_lo, 1)

                            for j in range(QT):
                                dve.wait_ge(s_g1[j], step * 16 + 16)
                                dve.wait_ge(s_a, step * QT + j + 1 + QT)
                                if j >= RT:
                                    dve.wait_ge(s_full, step + 1)
                                else:
                                    dve.wait_ge(s_lo, step * RT + j + 1)
                                V.tensor_tensor(pre[:, j, :], bank[j][:, :], gat[:, j, :], ALU.add).then_inc(s_add, 1)
                                dve.wait_ge(s_b1, (step + t) * QT + j + 5)
                                one_hot(hot_slot(j), quad_of(step, off) * QT + j, node_tile, s_hot1)
                                if j >= 1:
                                    low_part(j - 1)
                with dve.Fori(0, PAIRS) as i:
                    n = [l * NT + i * 2 + b for b in range(2)]
                    now = [h_now[:, bass.ds(i * 2 + b, 1), :].rearrange("p a n -> p (a n)") for b in range(2)]
                    for b in range(2):
                        if b == 0:
                            dve.wait_ge(s_acc1, l * NT + NT + 2)
                        V.scalar_tensor_tensor(g_in[:, b, :], now[b], eps_bc[:, bass.ds(l, 1)],
                                               sums[:, bass.ds(i * 2 + b, 1), 0:D].rearrange("p a n -> p (a n)"),
                                               ALU.mult, ALU.add).then_inc(s_gi, 1)
                    for b in range(2):
                        dve.wait_ge(s_z1, n[b] + 1)
                        dve.wait_ge(s_lw, l * (16 * 7) + 16 * 7)
                        V.tensor_tensor(z_in[:, b, :], bank[2 + b][:, :], b1_bc[:], ALU.add).then_inc(s_zi, 1)
                    for b in range(2):
                        dve.wait_ge(s_z2, n[b] + 1)
                        V.tensor_tensor(y_buf[:, b, :], bank[6 + b][:, :], b2_bc[:], ALU.add).then_inc(s_yb, 1)
                    for b in range(2):
                        dve.wait_ge(s_yr, n[b] + 1)
                        row_stats(b, y_buf[:, b, :], None, s_n1, n[b] * 5 - b * 3, s_var)
                    for b in range(2):
                        base = (l * NT + i * 2) * 5 + 4 + b * 3
                        dve.wait_ge(s_rs, n[b] + 1)
                        V.tensor_scalar(y_buf[:, b, :], y_buf[:, b, :], mean_var[:, b, 0:1], rstd[:, b:b + 1],
                                        ALU.subtract, ALU.mult).then_inc(s_n1, 1)
                        dve.wait_ge(s_n1, base + 1)
                        V.tensor_tensor(y_buf[:, b, :], y_buf[:, b, :], gamma_bc[:], ALU.mult).then_inc(s_n1, 1)
                        dve.wait_ge(s_n1, base + 2)
                        V.tensor_tensor(now[b], y_buf[:, b, :], beta_bc[:], ALU.add).then_inc(s_n1, 1)
                        dve.wait_ge(s_n1, base + 3)
                        V.tensor_tensor(sums[:, bass.ds(i * 2 + b, 1), D:2 * D].rearrange("p a n -> p (a n)"), now[b],
                                        be_bc[:], ALU.add).then_inc(s_rows, 1)

            with dve.Fori(0, PAIRS) as i:
                for b in range(2):
                    t = i * 2 + b
                    dve.wait_ge(s_fm, t + 1)
                    dve.wait_ge(s_frows, t + 1)
                    dve.wait_ge(s_wf, 32)
                    V.tensor_tensor(y_buf[:, b, :], bank[2 + b][:, :], b1_bc[:], ALU.add).then_inc(s_fn, 1)
                    dve.wait_ge(s_fn, t * 4 + 1)
                    V.tensor_tensor(y_buf[:, b, :], y_buf[:, b, :], h_first[:, bass.ds(t, 1), :]
                                    .rearrange("p a n -> p (a n)"), ALU.add).then_inc(s_fn, 1)
                    dve.wait_ge(s_fn, t * 4 + 2)
                    row_stats(b, y_buf[:, b, :], None, s_fn, t * 4 + 2, s_fvar)
                for b in range(2):
                    t = i * 2 + b
                    dve.wait_ge(s_frs, t + 1)
                    V.tensor_scalar(sums[:, bass.ds(t, 1), 0:D].rearrange("p a n -> p (a n)"), y_buf[:, b, :],
                                    mean_var[:, b, 0:1], rstd[:, b:b + 1], ALU.subtract, ALU.mult).then_inc(s_frows, 1)


def kernel(x, src, dst, edge_attr_128, edge_attr_4, edge_attr_8, L0_gnn_W_up0, L0_gnn_W_up1, L0_gnn_W_mlp1,
           L0_gnn_W_mlp2, L0_gnn_W_mlp3, L0_gnn_W_mlp4, L0_gnn_W_out0, L0_gnn_W_out1, L1_gnn_We, L1_gnn_be, L1_gnn_eps,
           L1_gnn_W1, L1_gnn_b1, L1_gnn_W2, L1_gnn_b2, L1_gnn_gamma, L1_gnn_beta, L1_gnn_Wf, L1_gnn_bf):
    import numpy as np
    import concourse.bacc as bacc
    from concourse.bass_utils import run_bass_kernel_spmd as run

    x, src, dst = np.asarray(x), np.asarray(src), np.asarray(dst)
    ea, y4, ef = np.asarray(edge_attr_128), np.asarray(edge_attr_4), np.asarray(edge_attr_8)
    n, d = x.shape
    e = src.shape[0]
    mul = d // 4
    node_pad = -n % P
    quads = -(-e // QE)
    pad = quads * QE - e

    xp = np.pad(x, ((0, node_pad), (0, 0)))
    planes = np.stack([xp[:, :mul].T] + [xp[:, mul + m::3].T for m in range(3)])
    efp = np.pad(ef, ((0, pad), (0, 0))).reshape(quads, 2, QE // 2, ef.shape[1])
    arrays = {
        "x": xp,
        "x_planes": planes,
        "src_t": np.pad(src, (0, pad)).reshape(-1, P).T,
        "dst_t": np.pad(dst, (0, pad + QE), constant_values=-1).reshape(-1, P).T,
        "ea_t": np.pad(ea, ((0, pad), (0, 0))).T,
        "ya": np.pad(y4, ((0, pad), (0, 0))).reshape(-1, P, 4).transpose(1, 0, 2).reshape(P, -1),
        "ef_t": efp.transpose(1, 3, 0, 2).reshape(2 * ef.shape[1], -1),
        "W_up0": L0_gnn_W_up0, "W_up1": L0_gnn_W_up1, "W_m1": L0_gnn_W_mlp1, "W_m2": L0_gnn_W_mlp2,
        "W_m3": L0_gnn_W_mlp3, "W_m4": L0_gnn_W_mlp4, "W_out0": L0_gnn_W_out0, "W_out1": L0_gnn_W_out1,
        "We": L1_gnn_We, "be": L1_gnn_be, "be_next": np.roll(np.asarray(L1_gnn_be), -1, axis=0), "eps": L1_gnn_eps,
        "W1": L1_gnn_W1, "b1": L1_gnn_b1, "W2": L1_gnn_W2, "b2": L1_gnn_b2, "gamma": L1_gnn_gamma,
        "beta": L1_gnn_beta, "Wf": L1_gnn_Wf, "bf": L1_gnn_bf,
    }
    arrays = {f"in_{k}": np.ascontiguousarray(v) for k, v in arrays.items()}
    nc = bacc.Bacc("TRN2", target_bir_lowering=False, num_devices=1)
    args = [nc.dram_tensor(k, v.shape, mybir.dt.from_np(v.dtype), kind="ExternalInput").ap() for k, v in arrays.items()]
    out = nc.dram_tensor("out_0", (n, d), F32, kind="ExternalOutput").ap()
    build(nc, *args, out)
    r = run(nc, [arrays], core_ids=[0])
    return r.results[0]["out_0"]
```
